# Optimizing a Trainium2 kernel written in Bass

```python
import numpy as np
import jax
import jax.numpy as jnp

def _softmax(x, axis=-1):
    return jax.nn.softmax(x, axis=axis)

def _gelu(x):
    return jax.nn.gelu(x, approximate=True)

def _silu(x):
    return jax.nn.silu(x)

def _sigmoid(x):
    return jax.nn.sigmoid(x)

def _layernorm(x, axis=-1, eps=1e-05):
    m = jnp.mean(x, axis=axis, keepdims=True)
    v = jnp.var(x, axis=axis, keepdims=True)
    return (x - m) / jnp.sqrt(v + eps)

def _scatter_add(tgt, idx, src, axis=0):
    return tgt.at[idx].add(src)

def _segment_sum(src, seg, n):
    return jax.ops.segment_sum(src, seg, n)
kernel_name = 'mk_rec_standalone_d1_rec_r8_fe6721'

def setup_inputs(seed: int=0):
    np.random.seed(seed)
    _w = jnp.asarray

    def _rec_inputs():
        import jax
        import jax.numpy as jnp
        _rk = jax.random.key(seed)
        r_idx = jax.random.randint(jax.random.fold_in(_rk, 1), (512, 16, 20), 0, 12500, jnp.int32)
        return r_idx
    r_idx = _rec_inputs()

    def _L0_rec_setup():
        import jax, jax.numpy as jnp
        import numpy as np
        NUM_TABLES = 16
        VOCAB = 12500
        EMBED_DIM = 64
        MLP_DIMS = [NUM_TABLES * EMBED_DIM, 512, 256, 1]
        key = jax.random.key(seed)
        k_idx, k_emb, *k_mlp = jax.random.split(key, 2 + 2 * (len(MLP_DIMS) - 1))
        idx = jax.random.randint(k_idx, (1024, NUM_TABLES, 20), 0, VOCAB, dtype=jnp.int64 if jax.config.read('jax_enable_x64') else jnp.int32)
        emb = jax.random.normal(k_emb, (NUM_TABLES, VOCAB, EMBED_DIM), dtype=jnp.float32) * 0.01
        Ws, bs = ([], [])
        for i, (d0, d1) in enumerate(zip(MLP_DIMS, MLP_DIMS[1:])):
            Ws.append(jax.random.normal(k_mlp[2 * i], (d0, d1), dtype=jnp.float32) * (1.0 / np.sqrt(d0)))
            bs.append(jax.random.normal(k_mlp[2 * i + 1], (d1,), dtype=jnp.float32) * 0.01)
        return {'idx': idx, 'emb': emb, 'W0': Ws[0], 'b0': bs[0], 'W1': Ws[1], 'b1': bs[1], 'W2': Ws[2], 'b2': bs[2]}
    _L0_rec_all = _L0_rec_setup()
    _L0_rec_in = {k: v for k, v in _L0_rec_all.items() if k in ('emb', 'W0', 'b0', 'W1', 'b1', 'W2', 'b2')}
    del _L0_rec_all
    return {'r_idx': r_idx, 'L0_rec_emb': _L0_rec_in['emb'], 'L0_rec_W0': _L0_rec_in['W0'], 'L0_rec_b0': _L0_rec_in['b0'], 'L0_rec_W1': _L0_rec_in['W1'], 'L0_rec_b1': _L0_rec_in['b1'], 'L0_rec_W2': _L0_rec_in['W2'], 'L0_rec_b2': _L0_rec_in['b2']}

def reference(r_idx, L0_rec_emb, L0_rec_W0, L0_rec_b0, L0_rec_W1, L0_rec_b1, L0_rec_W2, L0_rec_b2):
    import jax
    import jax.numpy as jnp

    def _L0_rec_ref(idx, emb, W0, b0, W1, b1, W2, b2):
        import jax, jax.numpy as jnp
        import numpy as np
        NUM_TABLES = 16
        VOCAB = 12500
        EMBED_DIM = 64
        MLP_DIMS = [NUM_TABLES * EMBED_DIM, 512, 256, 1]
        pooled = jax.vmap(lambda w, i: w[i].mean(axis=1), in_axes=(0, 1), out_axes=1)(emb, idx)
        B = pooled.shape[0]
        cat = pooled.reshape(B, -1)
        h = jax.nn.relu(cat @ W0 + b0)
        h = jax.nn.relu(h @ W1 + b1)
        out = h @ W2 + b2
        return out[:, 0]
    y = _L0_rec_ref(r_idx, L0_rec_emb, L0_rec_W0, L0_rec_b0, L0_rec_W1, L0_rec_b1, L0_rec_W2, L0_rec_b2)
    return y

_drawn_inputs = setup_inputs


def setup_inputs(seed=0):
    import zlib

    import numpy as np

    out = dict(_drawn_inputs(seed))
    spreads = {}
    factors = {}
    for name, (base, spread) in spreads.items():
        noise = np.random.default_rng([zlib.crc32(name.encode()), seed]).standard_normal(out[name].shape)
        drawn = base * np.exp(spread * noise) if base else spread * noise
        out[name] = jnp.asarray(drawn.astype(out[name].dtype))
    for name, factor in factors.items():
        out[name] = (out[name] * factor).astype(out[name].dtype)
    return out
```

```python
from contextlib import ExitStack

import concourse.bass as bass
from concourse import mybir

ALU = mybir.AluOpType
ACT = mybir.ActivationFunctionType
F32 = mybir.dt.float32
I32 = mybir.dt.int32
U32 = mybir.dt.uint32

P = 128
PARTS = 5


def embedding_bags_mlp(nc, r_idx, emb, W0, b0, W1, b1, W2, b2, out):
    B, T, J = r_idx.shape
    _, V, D = emb.shape
    H0, H1 = W0.shape[1], W1.shape[1]
    BT = B // P
    C = T // 2
    G = C * BT
    M0, M1 = H0 // P, H1 // P
    JP = J // PARTS
    PART_DONE = 16 * 2 * JP
    assert 2 * D == P and T % 2 == 0 and B % P == 0 and J % PARTS == 0 and G % 2 == 0

    rows_dram = emb.rearrange("t v d -> (t v) d")

    with ExitStack() as ctx:
        def sb(name, shape, dt):
            return ctx.enter_context(nc.sbuf_tensor(name, shape, dt))

        def psum(name):
            return ctx.enter_context(nc.psum_tensor(name, [P, 512], F32))

        def sem(name):
            return ctx.enter_context(nc.semaphore(name))

        idx_in = sb("idx_in", [P, C, BT, 2 * J], I32)
        table_start = sb("table_start", [P, C, BT, 2 * J], I32)
        idx_rows = sb("idx_rows", [P, G * 2 * J], I32)
        idx_now = sb("idx_now", [P, 2, 2 * J], I32)
        rows = sb("rows", [P, 2, J, 2 * D], F32)
        identity = sb("identity", [P, P], F32)
        feat = sb("feat", [P, G * P], F32)
        w0 = sb("w0", [P, C, H0], F32)
        w1 = sb("w1", [P, M0, H1], F32)
        w2 = sb("w2", [P, M1], F32)
        bias0 = sb("bias0", [P, M0], F32)
        bias1 = sb("bias1", [P, M1], F32)
        bias2 = sb("bias2", [1, 1], F32)
        h0 = sb("h0", [P, M0, B], F32)
        h1 = sb("h1", [P, M1, B], F32)
        y = sb("y", [1, B], F32)

        ps_bag = [psum("ps_bag0"), psum("ps_bag1")]
        ps_h0 = [psum("ps_h0_0"), psum("ps_h0_1")]
        ps_h1 = [psum("ps_h1_0"), psum("ps_h1_1")]
        ps_y = psum("ps_y")

        idx_landed = sem("idx_landed")
        starts_made = sem("starts_made")
        zeroed = sem("zeroed")
        identity_made = sem("identity_made")
        rows_made = sem("rows_made")
        idx_ready = sem("idx_ready")
        group_opened = sem("group_opened")
        landed = [[sem(f"landed{s}_{q}") for q in range(PARTS)] for s in range(2)]
        bag_summed = sem("bag_summed")
        bag_free = sem("bag_free")
        weights_landed = sem("weights_landed")
        h0_summed = sem("h0_summed")
        h0_ready = sem("h0_ready")
        h1_summed = sem("h1_summed")
        h1_ready = sem("h1_ready")
        y_summed = sem("y_summed")
        y_ready = sem("y_ready")
        out_landed = sem("out_landed")
        WEIGHT_LOADS = 6

        block = ctx.enter_context(nc.Block())

        @block.sync
        def _(sp):
            for t in range(BT):
                sp.dma_start(idx_in[:, :, t, :],
                             r_idx[t * P:(t + 1) * P].rearrange("p (c a) j -> p c (a j)", a=2)).then_inc(idx_landed, 16)
            sp.dma_start(w0[:], W0.rearrange("(c p) n -> p c n", p=P)).then_inc(weights_landed, 16)
            sp.dma_start(w1[:], W1.rearrange("(c p) n -> p c n", p=P)).then_inc(weights_landed, 16)
            with nc.allow_non_contiguous_dma(reason="a few hundred values, once"):
                sp.dma_start(bias0[:], b0.rearrange("(c p) -> p c", p=P)).then_inc(weights_landed, 16)
                sp.dma_start(bias1[:], b1.rearrange("(c p) -> p c", p=P)).then_inc(weights_landed, 16)
                sp.dma_start(w2[:], W2.rearrange("(c p) n -> p (c n)", p=P)).then_inc(weights_landed, 16)
            sp.dma_start(bias2[:], b2.rearrange("(a n) -> a n", a=1)).then_inc(weights_landed, 16)
            sp.wait_ge(y_ready, 1)
            sp.dma_start(out.rearrange("(a n) -> a n", a=1), y[:]).then_inc(out_landed, 16)
            sp.wait_ge(out_landed, 16)

        @block.gpsimd
        def _(pool):
            nc.gpsimd.iota(table_start[:], [[2 * V, C], [0, BT], [V, 2], [0, J]], base=0,
                           channel_multiplier=0).then_inc(starts_made, 1)
            nc.gpsimd.memset(identity[:], 0.0).then_inc(zeroed, 1)
            pool.wait_ge(zeroed, 1)
            nc.gpsimd.affine_select(out=identity[:], in_=identity[:], compare_op=ALU.not_equal, fill=1.0,
                                    base=0, pattern=[[-1, P]], channel_multiplier=1).then_inc(identity_made, 1)
            with pool.Fori(0, G // 2) as i:
                for s in range(2):
                    pool.wait_ge(idx_ready, 2 * i + s + 1)
                    pool.sem_inc(group_opened, 1)
                    for j in range(J):
                        for a in range(2):
                            nc.gpsimd.indirect_dma_start(
                                rows[:, s, j, a * D:(a + 1) * D], None, rows_dram,
                                bass.IndirectOffsetOnAxis(ap=idx_now[:, s, a * J + j:a * J + j + 1].bitcast(U32), axis=0),
                            ).then_inc(landed[s][j // JP], 16)

        @block.vector
        def _(dve):
            dve.wait_ge(idx_landed, 16 * BT)
            dve.wait_ge(starts_made, 1)
            nc.vector.tensor_tensor(idx_rows[:], idx_in[:].rearrange("p c t j -> p (c t j)"),
                                    table_start[:].rearrange("p c t j -> p (c t j)"), ALU.add).then_inc(rows_made, 1)
            dve.wait_ge(rows_made, 1)
            with dve.Fori(0, G // 2) as i:
                for s in range(2):
                    dve.wait_ge(bag_free, 2 * i + s + 1)
                    nc.vector.tensor_copy(idx_now[:, s, :],
                                          idx_rows[:, bass.ds((2 * i + s) * (2 * J), 2 * J)]).then_inc(idx_ready, 1)

        @block.tensor
        def _(pe):
            pe.wait_ge(identity_made, 1)
            with pe.Fori(0, G // 2) as i:
                for s in range(2):
                    pe.wait_ge(bag_free, 2 * i + s + 1)
                    for j in range(J):
                        if j % JP == 0:
                            pe.wait_ge(landed[s][j // JP], PART_DONE * (i + 1))
                        last = nc.tensor.matmul(ps_bag[s][:, 0:P], rows[:, s, j, :], identity[:],
                                                start=(j == 0), stop=(j == J - 1))
                    last.then_inc(bag_summed, 1)
            pe.wait_ge(weights_landed, 16 * WEIGHT_LOADS)
            pe.wait_ge(bag_free, G + 2)
            for m in range(M0):
                if m >= 2:
                    pe.wait_ge(h0_ready, m - 1)
                for c in range(C):
                    last = nc.tensor.matmul(ps_h0[m % 2][:, 0:B], w0[:, c, m * P:(m + 1) * P],
                                            feat[:, c * B:(c + 1) * B], start=(c == 0), stop=(c == C - 1))
                last.then_inc(h0_summed, 1)
            for m in range(M1):
                for c in range(M0):
                    pe.wait_ge(h0_ready, c + 1)
                    last = nc.tensor.matmul(ps_h1[m][:, 0:B], w1[:, c, m * P:(m + 1) * P], h0[:, c, :],
                                            start=(c == 0), stop=(c == M0 - 1))
                last.then_inc(h1_summed, 1)
            for c in range(M1):
                pe.wait_ge(h1_ready, c + 1)
                last = nc.tensor.matmul(ps_y[0:1, 0:B], w2[:, c:c + 1], h1[:, c, :],
                                        start=(c == 0), stop=(c == M1 - 1))
            last.then_inc(y_summed, 1)

        @block.scalar
        def _(act):
            act.sem_inc(bag_free, 2)
            with act.Fori(0, G // 2) as i:
                for s in range(2):
                    act.wait_ge(bag_summed, 2 * i + s + 1)
                    nc.scalar.activation(feat[:, bass.ds((2 * i + s) * P, P)], ps_bag[s][:, 0:P], ACT.Copy,
                                         scale=1.0 / J).then_inc(bag_free, 1)
            act.wait_ge(weights_landed, 16 * WEIGHT_LOADS)
            for m in range(M0):
                act.wait_ge(h0_summed, m + 1)
                nc.scalar.activation(h0[:, m, :], ps_h0[m % 2][:, 0:B], ACT.Relu,
                                     bias=bias0[:, m:m + 1]).then_inc(h0_ready, 1)
            for m in range(M1):
                act.wait_ge(h1_summed, m + 1)
                nc.scalar.activation(h1[:, m, :], ps_h1[m][:, 0:B], ACT.Relu,
                                     bias=bias1[:, m:m + 1]).then_inc(h1_ready, 1)
            act.wait_ge(y_summed, 1)
            nc.scalar.activation(y[:], ps_y[0:1, 0:B], ACT.Identity, bias=bias2[:]).then_inc(y_ready, 1)


_INS = ["r_idx", "L0_rec_emb", "L0_rec_W0", "L0_rec_b0", "L0_rec_W1", "L0_rec_b1", "L0_rec_W2", "L0_rec_b2"]


def kernel(**inputs):
    import numpy as _np
    import concourse.bacc as _bacc
    from concourse import mybir as _mybir
    from concourse.bass_utils import run_bass_kernel_spmd as _run

    nc = _bacc.Bacc("TRN2", target_bir_lowering=False, num_devices=1)
    arrays, args = {}, []
    for name in _INS:
        a = _np.ascontiguousarray(inputs[name])
        arrays[f"in_{name}"] = a
        args.append(nc.dram_tensor(f"in_{name}", a.shape, _mybir.dt.from_np(a.dtype), kind="ExternalInput").ap())
    n = inputs["r_idx"].shape[0]
    args.append(nc.dram_tensor("out_y", (n,), _mybir.dt.float32, kind="ExternalOutput").ap())
    embedding_bags_mlp(nc, *args)
    r = _run(nc, [arrays], core_ids=[0])
    return r.results[0]["out_y"]
```

```python
from contextlib import ExitStack

import concourse.bass as bass
from concourse import mybir

ALU = mybir.AluOpType
ACT = mybir.ActivationFunctionType
F32 = mybir.dt.float32
I32 = mybir.dt.int32
U32 = mybir.dt.uint32
BF16 = mybir.dt.bfloat16
F8E3 = mybir.dt.float8e3

P = 128
F8E3_ONE = 64.0


def embedding_bags_mlp(nc, r_idx, emb, W0, b0, W1, b1, W2, b2, out):
    B, T, J = r_idx.shape
    _, V, D = emb.shape
    H0, H1 = W0.shape[1], W1.shape[1]
    M0, M1 = H0 // P, H1 // P
    BT = B // P

    TD = 10
    TG = T - TD
    C = TG // 2
    G = C * BT
    JS = J // 2
    SLOT_ROWS = 2 * JS

    CH = -(-V // P)
    CH += CH % 2
    PC = 14
    NP = CH // PC
    F = 3
    Y = -(-B // (4 * F))
    YP = Y + Y % 2
    X = 2 * Y
    BH = F * X
    BS = 5
    STEPS = -(-Y // BS)
    assert 2 * D == P and B % P == 0 and TG % 2 == 0 and NP * PC == CH and PC % 2 == 0
    assert J < 32 and F * J <= 60 and BS * CH <= 512 and BH <= 512 and 2 * BH >= B
    assert (TD - 1) * V + CH * P <= T * V and V * T < 2 ** 24 and G >= TD
    assert STEPS <= 2 * NP

    SHIFT = 17
    MUL = 2 ** SHIFT // CH
    assert MUL * V < 2 ** 24 and all(v // CH - (v * MUL >> SHIFT) in (0, 1) for v in range(V))
    R6 = 2 * F
    MUL6, SHIFT6 = 10923, 16
    assert all(b // R6 == b * MUL6 >> SHIFT6 for b in range(B)) and R6 == 6

    emb_rows = emb.rearrange("t v d -> (t v) d")

    with ExitStack() as ctx:
        def sb(name, shape, dt):
            return ctx.enter_context(nc.sbuf_tensor(name, shape, dt))

        def psum(name):
            return ctx.enter_context(nc.psum_tensor(name, [P, 512], F32))

        def sem(name):
            return ctx.enter_context(nc.semaphore(name))

        counts = [sb(f"counts{hb}", [P, X, CH], I32) for hb in range(2)]
        count_bytes = [c[:].rearrange("p x h -> p (x h)").bitcast(F8E3)
                       .rearrange("p (x h f) -> p x h f", h=CH, f=4) for c in counts]
        values = sb("values", [P, 3, PC * D], F32)
        values_hi = [values[:, k, :].bitcast(BF16).rearrange("p (n w) -> p n w", w=2)[:, :, 1] for k in range(3)]
        rest = sb("rest", [P, 2, PC * D], F32)
        rest_hi = [rest[:, k, :].bitcast(BF16).rearrange("p (n w) -> p n w", w=2)[:, :, 1] for k in range(2)]
        hi_mid = sb("hi_mid", [P, NP, PC, 2, D], BF16)
        lo = sb("lo", [P, NP, PC * D], BF16)
        onehot_q = sb("onehot_q", [P, P, YP], BF16)
        onehot_h = sb("onehot_h", [P, CH, YP], BF16)
        number = sb("number", [P, P, YP], BF16)
        index_q = sb("index_q", [P, TD, 2 * YP], BF16)
        index_h = sb("index_h", [P, TD, 2 * YP], BF16)
        worth = sb("worth", [P, 1], F32)
        dense_sum = sb("dense_sum", [P, TD * 2 * BH], F32)
        rows = sb("rows", [P, 2, JS, 2 * D], F32)
        slot_sum = sb("slot_sum", [P, 2, 2 * D], F32)
        gathered_sum = sb("gathered_sum", [P, G * P], F32)
        identity = sb("identity", [P, P], F32)

        idx_in = sb("idx_in", [P, BT, T * J], I32)
        idx_rows = sb("idx_rows", [P, G * 2 * SLOT_ROWS], I32)
        idx_now = sb("idx_now", [P, 2, SLOT_ROWS], I32)
        part_no = sb("part_no", [P, 4], I32)
        part_f = sb("part_f", [P, 4], F32)
        bag_no = sb("bag_no", [P, 3, BT], I32)
        bag_f = sb("bag_f", [P, 2, BT], F32)
        residue = sb("residue", [P, BT, R6], F32)
        y_no = sb("y_no", [P, 2 * YP], F32)
        n_no = sb("n_no", [P, P], F32)
        choose_y = sb("choose_y", [P, BT, 2 * YP], BF16)

        w1 = sb("w1", [P, M0, H1], F32)
        w2 = sb("w2", [P, M1], F32)
        bias0 = sb("bias0", [P, M0], F32)
        bias1 = sb("bias1", [P, M1], F32)
        bias2 = sb("bias2", [1, 1], F32)
        y = sb("y", [1, B], F32)

        NI = BT * TD * J
        early = counts[1][:].rearrange("p x h -> p (x h)")
        int_a, int_b, int_c, int_d = (early[:, k * NI:(k + 1) * NI] for k in range(4))
        val_q, val_h = (early[:, (4 + k) * NI:(5 + k) * NI].bitcast(F32)
                        .rearrange("p (n t j) -> p n t j", n=BT, t=TD) for k in range(2))
        NS = BT * TD * P
        spread_words = counts[0][:].rearrange("p x h -> p (x h)")[:, 0:NS]
        spread = [spread_words[:, k * NS // 2:(k + 1) * NS // 2].bitcast(BF16)
                  .rearrange("p (n t c) -> p n t c", n=BT, t=TD) for k in range(2)]
        assert 6 * NI <= X * CH and NS <= X * CH
        late = counts[0][:].rearrange("p x h -> p (x h)").bitcast(F32)
        w0_dense = late[:, 0:TD * H0].rearrange("p (t n) -> p t n", n=H0)
        w0_gathered = late[:, TD * H0:(TD + C) * H0].rearrange("p (c n) -> p c n", n=H0)
        assert (TD + C) * H0 <= X * CH
        hidden = hi_mid[:].rearrange("p k c a d -> p (k c a d)").bitcast(F32)
        h0 = hidden[:, 0:M0 * B].rearrange("p (m b) -> p m b", b=B)
        h1 = hidden[:, M0 * B:(M0 + M1) * B].rearrange("p (m b) -> p m b", b=B)
        assert (M0 + M1) * B <= CH * D

        ps_sum = [psum(f"ps_sum{hb}") for hb in range(2)]
        ps_count = [[psum(f"ps_count{k}_{g}") for g in range(2)] for k in range(2)]
        ps_bag = psum("ps_bag")
        ps_y = psum("ps_y")
        ps_h0 = [ps_count[0][0], ps_count[0][1], ps_count[1][0], ps_count[1][1]]
        assert M0 == 4 and M1 == 2

        idx_landed = sem("idx_landed")
        numbers_made = sem("numbers_made")
        zeroed = sem("zeroed")
        identity_made = sem("identity_made")
        pads_zeroed = sem("pads_zeroed")
        gather_idx_made = sem("gather_idx_made")
        idx_copied = sem("idx_copied")
        group_opened = sem("group_opened")
        landed = [sem(f"landed{s}") for s in range(2)]
        slot_summed = sem("slot_summed")
        bag_summed = sem("bag_summed")
        bag_free = sem("bag_free")
        dve_step = sem("dve_step")
        qh_made = sem("qh_made")
        choice_made = sem("choice_made")
        spread_q_made = sem("spread_q_made")
        spread_h_made = sem("spread_h_made")
        turned = sem("turned")
        index_q_made = sem("index_q_made")
        index_h_made = sem("index_h_made")
        number_made = sem("number_made")
        worth_made = sem("worth_made")
        piece_landed = [sem(f"piece_landed{k}") for k in range(NP)]
        piece_used = sem("piece_used")
        rest_made = sem("rest_made")
        lo_made = sem("lo_made")
        hi_made = sem("hi_made")
        mid_made = sem("mid_made")
        onehot_h_made = sem("onehot_h_made")
        onehot_h_weighed = sem("onehot_h_weighed")
        onehot_q_made = sem("onehot_q_made")
        counted = sem("counted")
        kept = [sem("kept_act"), sem("kept_dve")]
        half_summed = sem("half_summed")
        half_kept = sem("half_kept")
        pe_gate = sem("pe_gate")
        weights_landed = sem("weights_landed")
        w0_landed = sem("w0_landed")
        h0_summed = sem("h0_summed")
        h0_ready = sem("h0_ready")
        h1_summed = sem("h1_summed")
        h1_ready = sem("h1_ready")
        y_summed = sem("y_summed")
        y_ready = sem("y_ready")
        out_landed = sem("out_landed")

        def table_piece(t, k):
            v = emb_rows[bass.ds(t * V, P * CH), :] if not isinstance(t, int) else emb_rows[t * V:t * V + P * CH, :]
            return v.rearrange("(p h) d -> p (h d)", h=CH)[:, k * PC * D:(k + 1) * PC * D]

        block = ctx.enter_context(nc.Block())

        @block.sync
        def _(sp):
            sp.dma_start(idx_in[:], r_idx.rearrange("(n p) t j -> p n (t j)", p=P)).then_inc(idx_landed, 16)
            def load_piece(t, k):
                if k == 0 and not (isinstance(t, int) and t == 0):
                    for taken in (rest_made, hi_made):
                        sp.wait_ge(taken, NP * t)
                elif k >= 3 or not (isinstance(t, int) and t == 0):
                    for taken in (rest_made, hi_made):
                        sp.wait_ge(taken, NP * t + k - 2)
                sp.dma_start(values[:, k % 3, :], table_piece(t, k)).then_inc(piece_landed[k], 16)

            for k in range(3):
                load_piece(0, k)
            sp.dma_start(w1[:], W1.rearrange("(c p) n -> p c n", p=P)).then_inc(weights_landed, 16)
            with nc.allow_non_contiguous_dma(reason="a few hundred values, once"):
                sp.dma_start(bias0[:], b0.rearrange("(c p) -> p c", p=P)).then_inc(weights_landed, 16)
                sp.dma_start(bias1[:], b1.rearrange("(c p) -> p c", p=P)).then_inc(weights_landed, 16)
                sp.dma_start(w2[:], W2.rearrange("(c p) n -> p (c n)", p=P)).then_inc(weights_landed, 16)
            sp.dma_start(bias2[:], b2.rearrange("(a n) -> a n", a=1)).then_inc(weights_landed, 16)
            for k in range(3, NP):
                load_piece(0, k)
            with sp.Fori(1, TD) as t:
                for k in range(NP):
                    load_piece(t, k)
            sp.wait_ge(half_summed, TD)
            for a in range(2):
                sp.dma_start(w0_dense[a * D:(a + 1) * D, :, :],
                             W0[0:TD * D].rearrange("(t p) n -> p t n", p=D)).then_inc(w0_landed, 16)
            sp.dma_start(w0_gathered, W0[TD * D:T * D].rearrange("(c p) n -> p c n", p=P)).then_inc(w0_landed, 16)
            sp.wait_ge(y_ready, 1)
            sp.dma_start(out.rearrange("(a n) -> a n", a=1), y[:]).then_inc(out_landed, 16)
            sp.wait_ge(out_landed, 16)

        @block.gpsimd
        def _(pool):
            nc.gpsimd.iota(bag_no[:, 0, :], [[P, BT]], base=0, channel_multiplier=1).then_inc(numbers_made, 1)
            nc.gpsimd.iota(part_no[:, 0:1], [[0, 1]], base=0, channel_multiplier=1).then_inc(numbers_made, 1)
            nc.gpsimd.iota(y_no[:], [[Y, 2], [1, YP]], base=0, channel_multiplier=0,
                           allow_small_or_imprecise_dtypes=True).then_inc(numbers_made, 1)
            nc.gpsimd.iota(n_no[:], [[1, P]], base=0, channel_multiplier=0,
                           allow_small_or_imprecise_dtypes=True).then_inc(numbers_made, 1)
            for k in range(2):
                for g in range(2):
                    nc.gpsimd.memset(spread[k][:, :, :, 64 * g + F * J:64 * g + 64], 0.0).then_inc(pads_zeroed, 1)
            nc.gpsimd.memset(identity[:], 0.0).then_inc(zeroed, 1)
            pool.wait_ge(zeroed, 1)
            nc.gpsimd.affine_select(out=identity[:], in_=identity[:], compare_op=ALU.not_equal, fill=1.0,
                                    base=0, pattern=[[-1, P]], channel_multiplier=1).then_inc(identity_made, 1)
            pool.wait_ge(gather_idx_made, TG)
            with pool.Fori(0, G) as i:
                for s in range(2):
                    pool.wait_ge(slot_summed, 2 * i + s + 1)
                    nc.gpsimd.tensor_copy(idx_now[:, s, :],
                                          idx_rows[:, bass.ds((2 * i + s) * SLOT_ROWS, SLOT_ROWS)]).then_inc(idx_copied, 1)
                    pool.wait_ge(idx_copied, 2 * i + s + 1)
                    pool.sem_inc(group_opened, 1)
                    for a in range(2):
                        for j in range(JS):
                            nc.gpsimd.indirect_dma_start(
                                rows[:, s, j, a * D:(a + 1) * D], None, emb_rows,
                                bass.IndirectOffsetOnAxis(
                                    ap=idx_now[:, s, a * JS + j:a * JS + j + 1].bitcast(U32), axis=0),
                            ).then_inc(landed[s], 16)

        @block.vector
        def _(dve):
            dve.wait_ge(idx_landed, 16)
            gi = idx_rows[:].rearrange("p (c n s a j) -> p c n s a j", c=C, n=BT, s=2, a=2)
            for t in range(TG):
                nc.vector.tensor_scalar(
                    gi[:, t // 2, :, :, t % 2, :],
                    idx_in[:, :, (TD + t) * J:(TD + t + 1) * J].rearrange("p n (s j) -> p n s j", s=2),
                    float((TD + t) * V), None, ALU.add).then_inc(gather_idx_made, 1)
            dense = idx_in[:, :, 0:TD * J]
            a3, b3, c3, d3 = (x.rearrange("p (n i) -> p n i", n=BT) for x in (int_a, int_b, int_c, int_d))
            nc.vector.tensor_scalar(a3, dense, float(MUL), None, ALU.mult).then_inc(dve_step, 1)
            dve.wait_ge(dve_step, 1)
            nc.vector.tensor_scalar(b3, a3, SHIFT, None, ALU.logical_shift_right).then_inc(dve_step, 1)
            dve.wait_ge(dve_step, 2)
            nc.vector.scalar_tensor_tensor(out=c3, in0=b3, scalar=float(-CH), in1=dense,
                                           op0=ALU.mult, op1=ALU.add).then_inc(dve_step, 1)
            dve.wait_ge(dve_step, 3)
            nc.vector.tensor_scalar(d3, c3, float(CH), None, ALU.is_ge).then_inc(dve_step, 1)
            dve.wait_ge(dve_step, 4)
            flat_q, flat_h = (x.rearrange("p n t j -> p (n t j)") for x in (val_q, val_h))
            nc.vector.scalar_tensor_tensor(out=flat_h, in0=int_d, scalar=float(-CH), in1=int_c,
                                           op0=ALU.mult, op1=ALU.add).then_inc(qh_made, 1)
            nc.vector.tensor_tensor(flat_q, int_b, int_d, ALU.add).then_inc(qh_made, 1)
            dve.wait_ge(numbers_made, 4)
            nc.vector.tensor_scalar(bag_no[:, 1, :], bag_no[:, 0, :], float(MUL6), None, ALU.mult).then_inc(dve_step, 1)
            dve.wait_ge(dve_step, 5)
            nc.vector.tensor_scalar(bag_no[:, 2, :], bag_no[:, 1, :], SHIFT6, None,
                                    ALU.logical_shift_right).then_inc(dve_step, 1)
            dve.wait_ge(dve_step, 6)
            nc.vector.tensor_copy(bag_f[:, 0, :], bag_no[:, 2, :]).then_inc(dve_step, 1)
            nc.vector.scalar_tensor_tensor(out=bag_f[:, 1, :], in0=bag_no[:, 2, :], scalar=float(-R6),
                                           in1=bag_no[:, 0, :], op0=ALU.mult, op1=ALU.add).then_inc(dve_step, 1)
            dve.wait_ge(dve_step, 8)
            for r in range(R6):
                nc.vector.tensor_scalar(residue[:, :, r], bag_f[:, 1, :], float(r), None,
                                        ALU.is_equal).then_inc(choice_made, 1)
            for n in range(BT):
                nc.vector.tensor_scalar(choose_y[:, n, :], y_no[:], bag_f[:, 0, n:n + 1], None,
                                        ALU.is_equal).then_inc(choice_made, 1)
            dve.wait_ge(qh_made, 2)
            dve.wait_ge(choice_made, R6 + BT)
            for n in range(BT):
                for r in range(R6):
                    c = 64 * (r // F) + J * (r % F)
                    nc.vector.tensor_scalar(spread[0][:, n, :, c:c + J], val_q[:, n, :, :], residue[:, n, r:r + 1],
                                            None, ALU.mult).then_inc(spread_q_made, 1)
            nc.vector.tensor_scalar(part_no[:, 1:2], part_no[:, 0:1], 63, None, ALU.bitwise_and).then_inc(dve_step, 1)
            dve.wait_ge(dve_step, 9)
            for f in (1, 2):
                nc.vector.tensor_scalar(part_f[:, f:f + 1], part_no[:, 1:2], float(J * f), float(256 ** f - 256 ** (f - 1)),
                                        ALU.is_ge, ALU.mult).then_inc(dve_step, 1)
            dve.wait_ge(dve_step, 11)
            nc.vector.scalar_tensor_tensor(out=worth[:], in0=part_f[:, 1:2], scalar=1.0, in1=part_f[:, 2:3],
                                           op0=ALU.add, op1=ALU.add).then_inc(worth_made, 1)

            def split(t, k):
                dve.wait_ge(piece_landed[k], 16 * t + 16)
                if k >= 2:
                    dve.wait_ge(mid_made, NP * t + k - 1)
                elif not isinstance(t, int) or t > 0:
                    dve.wait_ge(mid_made, NP * t)
                nc.vector.tensor_tensor(rest[:, k % 2, :], values[:, k % 3, :], values_hi[k % 3],
                                        ALU.subtract).then_inc(rest_made, 1)
                dve.wait_ge(rest_made, NP * t + k + 1)
                dve.wait_ge(piece_used, NP * t + k + 1)
                nc.vector.tensor_tensor(lo[:, k, :], rest[:, k % 2, :], rest_hi[k % 2],
                                        ALU.subtract).then_inc(lo_made, 1)

            def sum_slot(g, s):
                dve.wait_ge(landed[s], 16 * SLOT_ROWS * g + 16 * SLOT_ROWS)
                if not isinstance(g, int) or g > 0:
                    dve.wait_ge(bag_summed, g)
                nc.vector.tensor_reduce(slot_sum[:, s, :], rows[:, s, :, :].rearrange("p j e -> p e j"),
                                        axis=mybir.AxisListType.X, op=ALU.add).then_inc(slot_summed, 1)

            def one_hots(t, hb):
                if not (isinstance(t, int) and t == 0 and hb == 0):
                    dve.wait_ge(counted, (2 * t + hb) * STEPS)
                def of(index, n):
                    v = index[:, bass.ds(t, 1), hb * YP:(hb + 1) * YP] if not isinstance(t, int) \
                        else index[:, t:t + 1, hb * YP:(hb + 1) * YP]
                    return v.to_broadcast([P, n, YP])
                nc.vector.tensor_tensor(onehot_h[:], number[:, 0:CH, :], of(index_h, CH),
                                        ALU.is_equal).then_inc(onehot_h_made, 1)
                nc.vector.tensor_tensor(onehot_q[:], number[:], of(index_q, P),
                                        ALU.is_equal).then_inc(onehot_q_made, 1)

            def keep(t, hb, s):
                n = min(BS, Y - s * BS)
                dve.wait_ge(counted, (2 * t + hb) * STEPS + s + 1)
                nc.vector.tensor_copy(counts[hb][:, 2 * s * BS + 1:2 * (s * BS + n):2, :],
                                      ps_count[s % 2][1][:, 0:n * CH].rearrange("p (y h) -> p y h", h=CH)
                                      ).then_inc(kept[1], 1)

            dve.wait_ge(turned, 2)
            for k in range(2):
                nc.vector.tensor_copy(index_q[:, k * TD // 2:(k + 1) * TD // 2, :],
                                      ps_count[0][k][:, 0:TD * YP].rearrange("p (t y) -> p t y", y=2 * YP)
                                      ).then_inc(index_q_made, 1)
            dve.wait_ge(index_q_made, 2)
            dve.wait_ge(index_h_made, 2)
            dve.wait_ge(number_made, 1)
            one_hots(0, 0)
            for k in range(4):
                split(0, k)
            for s in range(STEPS):
                keep(0, 0, s)
            one_hots(0, 1)
            sum_slot(0, 0)
            sum_slot(0, 1)

            def table_steps(t, last):
                for s in range(STEPS):
                    keep(t, 1, s)
                    if s in (0, 2, 4):
                        split(t, 4 + s // 2)
                if not last:
                    one_hots(t + 1, 0)
                sum_slot(t + 1, 0)
                if not last:
                    for s in range(STEPS):
                        keep(t + 1, 0, s)
                        if s in (4, 6):
                            split(t + 1, (s - 4) // 2)
                    one_hots(t + 1, 1)
                    split(t + 1, 2)
                    split(t + 1, 3)
                sum_slot(t + 1, 1)

            with dve.Fori(0, TD - 1) as t:
                table_steps(t, False)
            table_steps(TD - 1, True)
            for g in range(TD + 1, G):
                sum_slot(g, 0)
                sum_slot(g, 1)

        @block.scalar
        def _(act):
            act.sem_inc(slot_summed, 2)
            act.sem_inc(bag_free, 1)
            act.sem_inc(half_kept, 2)
            act.sem_inc(piece_used, NP)
            act.wait_ge(numbers_made, 4)
            nc.scalar.activation(number[:], n_no[:].rearrange("p (n a) -> p n a", a=1).to_broadcast([P, P, YP]),
                                 ACT.Copy).then_inc(number_made, 1)
            act.wait_ge(qh_made, 2)
            act.wait_ge(choice_made, R6 + BT)
            for n in range(BT):
                for r in range(R6):
                    c = 64 * (r // F) + J * (r % F)
                    nc.scalar.activation(spread[1][:, n, :, c:c + J], val_h[:, n, :, :], ACT.Copy,
                                         scale=residue[:, n, r:r + 1]).then_inc(spread_h_made, 1)
            act.wait_ge(turned, 4)
            for k in range(2):
                nc.scalar.activation(index_h[:, k * TD // 2:(k + 1) * TD // 2, :],
                                     ps_count[1][k][:, 0:TD * YP].rearrange("p (t y) -> p t y", y=2 * YP),
                                     ACT.Copy).then_inc(index_h_made, 1)

            def weigh(t, hb):
                act.wait_ge(onehot_h_made, 2 * t + hb + 1)
                nc.scalar.activation(onehot_h[:], onehot_h[:], ACT.Copy, scale=worth[:, 0:1]).then_inc(onehot_h_weighed, 1)

            def split(t, k):
                act.wait_ge(piece_landed[k], 16 * t + 16)
                act.wait_ge(piece_used, NP * t + k + 1)
                nc.scalar.activation(hi_mid[:, k, :, 0, :], values_hi[k % 3].rearrange("p (c d) -> p c d", d=D),
                                     ACT.Copy).then_inc(hi_made, 1)
                act.wait_ge(rest_made, NP * t + k + 1)
                nc.scalar.activation(hi_mid[:, k, :, 1, :], rest_hi[k % 2].rearrange("p (c d) -> p c d", d=D),
                                     ACT.Copy).then_inc(mid_made, 1)

            def keep(t, hb, s):
                n = min(BS, Y - s * BS)
                act.wait_ge(counted, (2 * t + hb) * STEPS + s + 1)
                nc.scalar.activation(counts[hb][:, 2 * s * BS:2 * (s * BS + n) - 1:2, :],
                                     ps_count[s % 2][0][:, 0:n * CH].rearrange("p (y h) -> p y h", h=CH),
                                     ACT.Copy).then_inc(kept[0], 1)

            def keep_sum(t, hb):
                if hb == 0:
                    act.wait_ge(half_summed, t + 1)
                else:
                    act.wait_ge(piece_used, NP * t + 2 * NP)
                at = (2 * t + hb) * BH
                dst = dense_sum[:, bass.ds(at, BH)] if not isinstance(t, int) else dense_sum[:, at:at + BH]
                nc.scalar.activation(dst, ps_sum[hb][:, 0:BH], ACT.Copy, scale=F8E3_ONE / J).then_inc(half_kept, 1)

            def keep_bag(g):
                act.wait_ge(bag_summed, g + 1)
                dst = gathered_sum[:, bass.ds(g * P, P)] if not isinstance(g, int) else gathered_sum[:, g * P:(g + 1) * P]
                nc.scalar.activation(dst, ps_bag[:, 0:P], ACT.Copy, scale=1.0 / J).then_inc(bag_free, 1)

            act.wait_ge(worth_made, 1)
            weigh(0, 0)
            for k in range(4):
                split(0, k)
            for s in range(STEPS):
                keep(0, 0, s)
            weigh(0, 1)

            def table_steps(t, last):
                for s in range(STEPS):
                    keep(t, 1, s)
                    if s in (0, 2, 4):
                        split(t, 4 + s // 2)
                if not last:
                    weigh(t + 1, 0)
                keep_bag(t)
                keep_sum(t, 0)
                if not last:
                    for s in range(STEPS):
                        keep(t + 1, 0, s)
                        if s in (4, 6):
                            split(t + 1, (s - 4) // 2)
                    weigh(t + 1, 1)
                    split(t + 1, 2)
                    split(t + 1, 3)
                keep_sum(t, 1)

            with act.Fori(0, TD - 1) as t:
                table_steps(t, False)
            table_steps(TD - 1, True)
            for g in range(TD, G):
                keep_bag(g)

            act.wait_ge(weights_landed, 16 * 5)
            for m in range(M0):
                act.wait_ge(h0_summed, m + 1)
                nc.scalar.activation(h0[:, m, :], ps_h0[m][:, 0:B], ACT.Relu,
                                     bias=bias0[:, m:m + 1]).then_inc(h0_ready, 1)
            for m in range(M1):
                act.wait_ge(h1_summed, m + 1)
                nc.scalar.activation(h1[:, m, :], ps_sum[m][:, 0:B], ACT.Relu,
                                     bias=bias1[:, m:m + 1]).then_inc(h1_ready, 1)
            act.wait_ge(y_summed, 1)
            nc.scalar.activation(y[:], ps_y[0:1, 0:B], ACT.Identity, bias=bias2[:]).then_inc(y_ready, 1)

        @block.tensor
        def _(pe):
            for kind, made in ((0, spread_q_made), (1, spread_h_made)):
                pe.wait_ge(pads_zeroed, 4)
                pe.wait_ge(choice_made, R6 + BT)
                pe.wait_ge(made, BT * R6)
                for t in range(TD):
                    bank = ps_count[kind][t // (TD // 2)]
                    at = t % (TD // 2) * 2 * YP
                    for n in range(BT):
                        last = nc.tensor.matmul(bank[:, at:at + 2 * YP], spread[kind][:, n, t, :], choose_y[:, n, :],
                                                start=(n == 0), stop=(n == BT - 1))
                    if t % (TD // 2) == TD // 2 - 1:
                        last.then_inc(turned, 1)

            def count(t, hb, s):
                n = min(BS, Y - s * BS)
                if s == 0:
                    pe.wait_ge(onehot_h_weighed, 2 * t + hb + 1)
                    pe.wait_ge(onehot_q_made, 2 * t + hb + 1)
                if s >= 2:
                    for k in kept:
                        pe.wait_ge(k, (2 * t + hb) * STEPS + s - 1)
                for yy in range(n):
                    for g in range(2):
                        last = nc.tensor.matmul(ps_count[s % 2][g][:, yy * CH:(yy + 1) * CH],
                                                onehot_q[64 * g:64 * g + F * J, :, s * BS + yy],
                                                onehot_h[64 * g:64 * g + F * J, :, s * BS + yy],
                                                start=True, stop=True)
                last.then_inc(counted, 1)

            def turn_bags(g):
                pe.wait_ge(slot_summed, 2 * g + 4)
                pe.wait_ge(bag_free, g + 1)
                for s in range(2):
                    last = nc.tensor.matmul(ps_bag[:, 0:P], slot_sum[:, s, :], identity[:],
                                            start=(s == 0), stop=(s == 1))
                last.then_inc(bag_summed, 1)

            def half(t, hb, following):
                for k in kept:
                    pe.wait_ge(k, (2 * t + hb + 1) * STEPS)
                    pe.sem_inc(pe_gate, 1)
                pe.wait_ge(half_kept, 2 * t + hb + 1)
                pe.sem_inc(pe_gate, 1)
                for k in range(NP):
                    if following is not None and 2 * k < STEPS:
                        count(*following, 2 * k)
                    if hb == 0:
                        for made in (mid_made, lo_made):
                            pe.wait_ge(made, NP * t + k + 1)
                            pe.sem_inc(pe_gate, 1)
                    for c in range(PC):
                        nc.tensor.matmul(ps_sum[hb][:, 0:BH], hi_mid[:, k, c, :, :].rearrange("p a d -> p (a d)"),
                                         count_bytes[hb][:, :, k * PC + c, 0:F],
                                         start=(k == 0 and c == 0), stop=False)
                    if following is not None and 2 * k + 1 < STEPS:
                        count(*following, 2 * k + 1)
                    if hb == 0 and k == NP - 2:
                        turn_bags(t)
                    for c in range(PC):
                        odd = c % 2
                        last = nc.tensor.matmul(ps_sum[hb][odd * D:(odd + 1) * D, 0:BH], lo[:, k, c * D:(c + 1) * D],
                                                count_bytes[hb][:, :, k * PC + c, 0:F],
                                                start=False, stop=(k == NP - 1 and c >= PC - 2))
                    if hb == 1:
                        last.then_inc(piece_used, 1)
                    elif k == NP - 1:
                        last.then_inc(half_summed, 1)

            pe.wait_ge(index_q_made, 2)
            pe.wait_ge(index_h_made, 2)
            pe.wait_ge(identity_made, 1)
            for s in range(STEPS):
                count(0, 0, s)

            with pe.Fori(0, TD - 1) as t:
                half(t, 0, (t, 1))
                half(t, 1, (t + 1, 0))
            half(TD - 1, 0, (TD - 1, 1))
            half(TD - 1, 1, None)

            pe.wait_ge(w0_landed, 16 * 3)
            pe.wait_ge(half_kept, 2 * TD + 2)
            for m in range(M0):
                for t in range(TD):
                    nc.tensor.matmul(ps_h0[m][:, 0:B], w0_dense[:, t, m * P:(m + 1) * P],
                                     dense_sum[:, t * 2 * BH:t * 2 * BH + B], start=(t == 0), stop=False)

            def add_group(g):
                c, n = g // BT, g % BT
                pe.wait_ge(bag_free, g + 2)
                for m in range(M0):
                    last = nc.tensor.matmul(ps_h0[m][:, n * P:(n + 1) * P], w0_gathered[:, c, m * P:(m + 1) * P],
                                            gathered_sum[:, g * P:(g + 1) * P], start=False, stop=(g == G - 1))
                    if g == G - 1:
                        last.then_inc(h0_summed, 1)

            for g in range(TD):
                add_group(g)
            for g in range(TD, G):
                turn_bags(g)
                add_group(g)
            pe.wait_ge(weights_landed, 16 * 5)
            for m in range(M1):
                for c in range(M0):
                    pe.wait_ge(h0_ready, c + 1)
                    last = nc.tensor.matmul(ps_sum[m][:, 0:B], w1[:, c, m * P:(m + 1) * P], h0[:, c, :],
                                            start=(c == 0), stop=(c == M0 - 1))
                last.then_inc(h1_summed, 1)
            for c in range(M1):
                pe.wait_ge(h1_ready, c + 1)
                last = nc.tensor.matmul(ps_y[0:1, 0:B], w2[:, c:c + 1], h1[:, c, :],
                                        start=(c == 0), stop=(c == M1 - 1))
            last.then_inc(y_summed, 1)


_INS = ["r_idx", "L0_rec_emb", "L0_rec_W0", "L0_rec_b0", "L0_rec_W1", "L0_rec_b1", "L0_rec_W2", "L0_rec_b2"]


def kernel(**inputs):
    import numpy as _np
    import concourse.bacc as _bacc
    from concourse import mybir as _mybir
    from concourse.bass_utils import run_bass_kernel_spmd as _run

    nc = _bacc.Bacc("TRN2", target_bir_lowering=False, num_devices=1)
    arrays, args = {}, []
    for name in _INS:
        a = _np.ascontiguousarray(inputs[name])
        arrays[f"in_{name}"] = a
        args.append(nc.dram_tensor(f"in_{name}", a.shape, _mybir.dt.from_np(a.dtype), kind="ExternalInput").ap())
    n = inputs["r_idx"].shape[0]
    args.append(nc.dram_tensor("out_y", (n,), _mybir.dt.float32, kind="ExternalOutput").ap())
    embedding_bags_mlp(nc, *args)
    r = _run(nc, [arrays], core_ids=[0])
    return r.results[0]["out_y"]
```

```python
from contextlib import ExitStack

import concourse.bass as bass
from concourse import mybir

ALU = mybir.AluOpType
ACT = mybir.ActivationFunctionType
F32 = mybir.dt.float32
I32 = mybir.dt.int32
U32 = mybir.dt.uint32
BF16 = mybir.dt.bfloat16
F8E3 = mybir.dt.float8e3

P = 128
F8E3_ONE = 64.0


def embedding_bags_mlp(nc, r_idx, emb, W0, b0, W1, b1, W2, b2, out):
    B, T, J = r_idx.shape
    _, V, D = emb.shape
    H0, H1 = W0.shape[1], W1.shape[1]
    M0, M1 = H0 // P, H1 // P
    BT = B // P

    TD = 10
    TU = TD // 2
    TG = T - TD
    C = TG // 2
    G = C * BT
    JS = J // 2
    SLOT_ROWS = 2 * JS

    CH = -(-V // P)
    CH += CH % 2
    PC = 14
    NP = CH // PC
    F = 3
    Y = -(-B // (4 * F))
    YP = Y + Y % 2
    X = 2 * Y
    BH = F * X
    BS = 5
    STEPS = -(-Y // BS)
    ACT_STEPS = (3, 5, 7)
    DVE_STEPS = STEPS - len(ACT_STEPS)
    EARLY = 4
    SPLIT_AFTER = ((1, 3, 5), (1, 3, 5))
    COUNT_AT = 2
    assert 2 * D == P and B % P == 0 and TG % 2 == 0 and TD % 2 == 0 and NP * PC == CH and PC % 2 == 0
    assert J < 32 and F * J <= 60 and BS * CH <= 512 and BH <= 512 and 2 * BH >= B and TU * 2 * YP <= 512
    assert (TD - 1) * V + CH * P <= T * V and V * T < 2 ** 24 and G >= TD
    assert STEPS + COUNT_AT <= 2 * NP and len(SPLIT_AFTER[0]) == NP - EARLY and len(SPLIT_AFTER[1]) <= EARLY
    SUM_AFTER = (2, 2)
    TURN_AT = 0
    R6_DVE = 4

    QSHIFT = 10
    assert all(int((v + 0.5) * 2 ** QSHIFT / CH) + r >> QSHIFT == v // CH for v in range(V) for r in (-1, 0, 1, 2))
    R6 = 2 * F
    MUL6, SHIFT6 = 10923, 16
    assert all(b // R6 == b * MUL6 >> SHIFT6 for b in range(B)) and R6 == 6

    emb_rows = emb.rearrange("t v d -> (t v) d")

    with ExitStack() as ctx:
        def sb(name, shape, dt):
            return ctx.enter_context(nc.sbuf_tensor(name, shape, dt))

        def psum(name):
            return ctx.enter_context(nc.psum_tensor(name, [P, 512], F32))

        def sem(name):
            return ctx.enter_context(nc.semaphore(name))

        counts = [sb(f"counts{hb}", [P, X, CH], I32) for hb in range(2)]
        count_bytes = [c[:].rearrange("p x h -> p (x h)").bitcast(F8E3)
                       .rearrange("p (x h f) -> p x h f", h=CH, f=4) for c in counts]
        values = sb("values", [P, 3, PC * D], F32)
        values_hi = [values[:, k, :].bitcast(BF16).rearrange("p (n w) -> p n w", w=2)[:, :, 1] for k in range(3)]
        rest = sb("rest", [P, 2, PC * D], F32)
        rest_hi = [rest[:, k, :].bitcast(BF16).rearrange("p (n w) -> p n w", w=2)[:, :, 1] for k in range(2)]
        hi_mid = sb("hi_mid", [P, NP, PC, 2, D], BF16)
        lo = sb("lo", [P, NP, PC * D], BF16)
        onehot_q = sb("onehot_q", [P, P, YP], BF16)
        onehot_h = sb("onehot_h", [P, CH, YP], BF16)
        number = sb("number", [P, P, YP], BF16)
        index_q = sb("index_q", [P, TD, 2 * YP], BF16)
        index_h = sb("index_h", [P, TD, 2 * YP], BF16)
        worth = sb("worth", [P, 1], F32)
        part_sum = sb("part_sum", [P, 2, BH], F32)
        dense_sum = sb("dense_sum", [P, TD // 2 * 2 * BH], F32)
        rows = sb("rows", [P, 2, JS, 2 * D], F32)
        slot_sum = sb("slot_sum", [P, 2, 2 * D], F32)
        gathered_sum = sb("gathered_sum", [P, G * P], F32)
        identity = sb("identity", [P, P], F32)

        idx_in = sb("idx_in", [P, BT, T * J], I32)
        idx_rows = sb("idx_rows", [P, G * 2 * SLOT_ROWS], I32)
        idx_now = sb("idx_now", [P, 2, SLOT_ROWS], I32)
        part_no = sb("part_no", [P, 4], I32)
        part_f = sb("part_f", [P, 4], F32)
        bag_no = sb("bag_no", [P, 3, BT], I32)
        bag_f = sb("bag_f", [P, 2, BT], F32)
        residue = sb("residue", [P, BT, R6], F32)
        y_no = sb("y_no", [P, 2 * YP], F32)
        n_no = sb("n_no", [P, P], F32)
        choose_y = sb("choose_y", [P, BT, 2 * YP], F32)

        w1 = sb("w1", [P, M0, H1], F32)
        w2 = sb("w2", [P, M1], F32)
        bias0 = sb("bias0", [P, M0], F32)
        bias1 = sb("bias1", [P, M1], F32)
        bias2 = sb("bias2", [1, 1], F32)
        y = sb("y", [1, B], F32)

        NS = BT * TD * P
        spread = counts[1][:].rearrange("p x h -> p (x h)").bitcast(F32)[:, 0:NS].rearrange(
            "p (n t c) -> p n t c", n=BT, t=TD)
        NI = TU * 2 * YP
        steps_q = dense_sum[:].bitcast(I32)
        int_a, int_q = steps_q[:, 0:NI], steps_q[:, NI:2 * NI]
        assert NS <= X * CH and 2 * NI <= TU * 2 * BH
        late = counts[0][:].rearrange("p x h -> p (x h)").bitcast(F32)
        w0_dense = late[:, 0:TU * H0].rearrange("p (t n) -> p t n", n=H0)
        w0_gathered = late[:, TU * H0:(TU + C) * H0].rearrange("p (c n) -> p c n", n=H0)
        assert (TU + C) * H0 <= X * CH
        hidden = hi_mid[:].rearrange("p k c a d -> p (k c a d)").bitcast(F32)
        h0 = hidden[:, 0:M0 * B].rearrange("p (m b) -> p m b", b=B)
        h1 = hidden[:, M0 * B:(M0 + M1) * B].rearrange("p (m b) -> p m b", b=B)
        assert (M0 + M1) * B <= CH * D

        ps_sum = [psum(f"ps_sum{hb}") for hb in range(2)]
        ps_count = [[psum(f"ps_count{k}_{g}") for g in range(2)] for k in range(2)]
        ps_bag = psum("ps_bag")
        ps_y = psum("ps_y")
        ps_h0 = [ps_count[0][0], ps_count[0][1], ps_count[1][0], ps_count[1][1]]
        INDEX_PARTS = ((0, 1, ps_y), (1, 1 + TU, ps_bag), (1 + TU, TD, ps_sum[1]))
        assert M0 == 4 and M1 == 2

        idx_landed = sem("idx_landed")
        gather_idx_landed = sem("gather_idx_landed")
        numbers_made = sem("numbers_made")
        zeroed = sem("zeroed")
        identity_made = sem("identity_made")
        pads_zeroed = sem("pads_zeroed")
        gather_idx_made = sem("gather_idx_made")
        idx_copied = sem("idx_copied")
        group_opened = sem("group_opened")
        landed = [sem(f"landed{s}") for s in range(2)]
        slot_summed = sem("slot_summed")
        bag_summed = sem("bag_summed")
        bag_free = sem("bag_free")
        dve_step = sem("dve_step")
        choice_made = sem("choice_made")
        spread_made = sem("spread_made")
        turned = sem("turned")
        q_made = sem("q_made")
        index_q_made = sem("index_q_made")
        index_h_made = sem("index_h_made")
        number_made = sem("number_made")
        worth_made = sem("worth_made")
        piece_landed = [sem(f"piece_landed{k}") for k in range(NP)]
        piece_used = sem("piece_used")
        rest_made = sem("rest_made")
        lo_made = sem("lo_made")
        hi_made = sem("hi_made")
        mid_made = sem("mid_made")
        onehot_h_made = sem("onehot_h_made")
        onehot_h_weighed = sem("onehot_h_weighed")
        onehot_q_made = sem("onehot_q_made")
        counted = sem("counted")
        kept = [sem("kept_act"), sem("kept_dve")]
        half_summed = sem("half_summed")
        part_kept = sem("part_kept")
        half_kept = sem("half_kept")
        pe_gate = sem("pe_gate")
        weights_landed = sem("weights_landed")
        w0_landed = sem("w0_landed")
        h0_summed = sem("h0_summed")
        h0_ready = sem("h0_ready")
        h1_summed = sem("h1_summed")
        h1_ready = sem("h1_ready")
        y_summed = sem("y_summed")
        y_ready = sem("y_ready")
        out_landed = sem("out_landed")

        def table_piece(t, k):
            v = emb_rows[bass.ds(t * V, P * CH), :] if not isinstance(t, int) else emb_rows[t * V:t * V + P * CH, :]
            return v.rearrange("(p h) d -> p (h d)", h=CH)[:, k * PC * D:(k + 1) * PC * D]

        block = ctx.enter_context(nc.Block())

        @block.sync
        def _(sp):
            for tables, arrived in ((slice(TD * J, T * J), gather_idx_landed), (slice(0, TD * J), idx_landed)):
                sp.dma_start(idx_in[:, :, tables],
                             r_idx.rearrange("(n p) t j -> p n (t j)", p=P)[:, :, tables]).then_inc(arrived, 16)
            def load_piece(t, k):
                if k == 0 and not (isinstance(t, int) and t == 0):
                    for taken in (rest_made, hi_made):
                        sp.wait_ge(taken, NP * t)
                elif k >= 3 or not (isinstance(t, int) and t == 0):
                    for taken in (rest_made, hi_made):
                        sp.wait_ge(taken, NP * t + k - 2)
                sp.dma_start(values[:, k % 3, :], table_piece(t, k)).then_inc(piece_landed[k], 16)

            for k in range(3):
                load_piece(0, k)
            sp.dma_start(w1[:], W1.rearrange("(c p) n -> p c n", p=P)).then_inc(weights_landed, 16)
            with nc.allow_non_contiguous_dma(reason="a few hundred values, once"):
                sp.dma_start(bias0[:], b0.rearrange("(c p) -> p c", p=P)).then_inc(weights_landed, 16)
                sp.dma_start(bias1[:], b1.rearrange("(c p) -> p c", p=P)).then_inc(weights_landed, 16)
                sp.dma_start(w2[:], W2.rearrange("(c p) n -> p (c n)", p=P)).then_inc(weights_landed, 16)
            sp.dma_start(bias2[:], b2.rearrange("(a n) -> a n", a=1)).then_inc(weights_landed, 16)
            for k in range(3, NP):
                load_piece(0, k)
            with sp.Fori(1, TD) as t:
                for k in range(NP):
                    load_piece(t, k)
            sp.wait_ge(half_summed, TD)
            for a in range(2):
                sp.dma_start(w0_dense[a * D:(a + 1) * D, :, :],
                             W0[a * TU * D:(a + 1) * TU * D].rearrange("(t p) n -> p t n", p=D)).then_inc(w0_landed, 16)
            sp.dma_start(w0_gathered, W0[TD * D:T * D].rearrange("(c p) n -> p c n", p=P)).then_inc(w0_landed, 16)
            sp.wait_ge(y_ready, 2)
            sp.dma_start(out.rearrange("(a n) -> a n", a=1), y[:]).then_inc(out_landed, 16)
            sp.wait_ge(out_landed, 16)

        @block.gpsimd
        def _(pool):
            nc.gpsimd.iota(bag_no[:, 0, :], [[P, BT]], base=0, channel_multiplier=1).then_inc(numbers_made, 1)
            nc.gpsimd.iota(part_no[:, 0:1], [[0, 1]], base=0, channel_multiplier=1).then_inc(numbers_made, 1)
            nc.gpsimd.iota(y_no[:], [[Y, 2], [1, YP]], base=0, channel_multiplier=0,
                           allow_small_or_imprecise_dtypes=True).then_inc(numbers_made, 1)
            nc.gpsimd.iota(n_no[:], [[1, P]], base=0, channel_multiplier=0,
                           allow_small_or_imprecise_dtypes=True).then_inc(numbers_made, 1)
            for g in range(2):
                nc.gpsimd.memset(spread[:, :, :, 64 * g + F * J:64 * g + 64], 0.0).then_inc(pads_zeroed, 1)
            nc.gpsimd.memset(identity[:], 0.0).then_inc(zeroed, 1)
            pool.wait_ge(zeroed, 1)
            nc.gpsimd.affine_select(out=identity[:], in_=identity[:], compare_op=ALU.not_equal, fill=1.0,
                                    base=0, pattern=[[-1, P]], channel_multiplier=1).then_inc(identity_made, 1)
            with pool.Fori(0, G) as i:
                for s in range(2):
                    pool.wait_ge(slot_summed, 2 * i + s + 1)
                    pool.wait_ge(idx_copied, 2 * i + s + 1)
                    pool.sem_inc(group_opened, 1)
                    for a in range(2):
                        for j in range(JS):
                            nc.gpsimd.indirect_dma_start(
                                rows[:, s, j, a * D:(a + 1) * D], None, emb_rows,
                                bass.IndirectOffsetOnAxis(
                                    ap=idx_now[:, s, a * JS + j:a * JS + j + 1].bitcast(U32), axis=0),
                            ).then_inc(landed[s], 16)

        @block.vector
        def _(dve):
            def next_indices(g, s):
                at = (2 * g + s) * SLOT_ROWS
                src = idx_rows[:, bass.ds(at, SLOT_ROWS)] if not isinstance(g, int) else idx_rows[:, at:at + SLOT_ROWS]
                nc.vector.tensor_copy(idx_now[:, s, :], src).then_inc(idx_copied, 1)

            dve.wait_ge(numbers_made, 4)
            nc.vector.tensor_scalar(bag_no[:, 1, :], bag_no[:, 0, :], float(MUL6), None, ALU.mult).then_inc(dve_step, 1)
            dve.wait_ge(dve_step, 1)
            nc.vector.tensor_scalar(bag_no[:, 2, :], bag_no[:, 1, :], SHIFT6, None,
                                    ALU.logical_shift_right).then_inc(dve_step, 1)
            dve.wait_ge(dve_step, 2)
            nc.vector.tensor_copy(bag_f[:, 0, :], bag_no[:, 2, :]).then_inc(dve_step, 1)
            nc.vector.scalar_tensor_tensor(out=bag_f[:, 1, :], in0=bag_no[:, 2, :], scalar=float(-R6),
                                           in1=bag_no[:, 0, :], op0=ALU.mult, op1=ALU.add).then_inc(dve_step, 1)
            dve.wait_ge(dve_step, 4)
            for r in range(R6):
                nc.vector.tensor_scalar(residue[:, :, r], bag_f[:, 1, :], float(r), None,
                                        ALU.is_equal).then_inc(choice_made, 1)
            for n in range(BT):
                nc.vector.tensor_scalar(choose_y[:, n, :], y_no[:], bag_f[:, 0, n:n + 1], None,
                                        ALU.is_equal).then_inc(choice_made, 1)

            gi = idx_rows[:].rearrange("p (c n s a j) -> p c n s a j", c=C, n=BT, s=2, a=2)
            def gather_indices(t):
                nc.vector.tensor_scalar(
                    gi[:, t // 2, :, :, t % 2, :],
                    idx_in[:, :, (TD + t) * J:(TD + t + 1) * J].rearrange("p n (s j) -> p n s j", s=2),
                    float((TD + t) * V), None, ALU.add).then_inc(gather_idx_made, 1)

            dve.wait_ge(gather_idx_landed, 16)
            gather_indices(0)
            gather_indices(1)
            dve.wait_ge(gather_idx_made, 2)
            next_indices(0, 0)
            next_indices(0, 1)
            dve.wait_ge(idx_landed, 16)
            dve.wait_ge(choice_made, R6 + BT)
            for n in range(BT):
                for r in range(R6_DVE):
                    c = 64 * (r // F) + J * (r % F)
                    nc.vector.tensor_scalar(spread[:, n, :, c:c + J],
                                            idx_in[:, n, 0:TD * J].rearrange("p (t j) -> p t j", t=TD),
                                            residue[:, n, r:r + 1], None, ALU.mult).then_inc(spread_made, 1)
            nc.vector.tensor_scalar(part_no[:, 1:2], part_no[:, 0:1], 63, None, ALU.bitwise_and).then_inc(dve_step, 1)
            dve.wait_ge(dve_step, 5)
            for f in (1, 2):
                nc.vector.tensor_scalar(part_f[:, f:f + 1], part_no[:, 1:2], float(J * f), float(256 ** f - 256 ** (f - 1)),
                                        ALU.is_ge, ALU.mult).then_inc(dve_step, 1)
            dve.wait_ge(dve_step, 7)
            nc.vector.scalar_tensor_tensor(out=worth[:], in0=part_f[:, 1:2], scalar=1.0, in1=part_f[:, 2:3],
                                           op0=ALU.add, op1=ALU.add).then_inc(worth_made, 1)

            def find_qh(i):
                t0, t1, bank = INDEX_PARTS[i]
                n = (t1 - t0) * 2 * YP
                v = bank[:, 0:n]
                dve.wait_ge(turned, i + 1)
                if i > 0:
                    dve.wait_ge(index_q_made, i)
                nc.vector.tensor_scalar(int_a[:, 0:n], v, 0.5, 2.0 ** QSHIFT / CH, ALU.add, ALU.mult).then_inc(dve_step, 1)
                dve.wait_ge(dve_step, 8 + i)
                nc.vector.tensor_scalar(int_q[:, 0:n], int_a[:, 0:n], QSHIFT, None,
                                        ALU.logical_shift_right).then_inc(q_made, 1)
                dve.wait_ge(q_made, i + 1)
                nc.vector.scalar_tensor_tensor(out=index_h[:, t0:t1, :].rearrange("p t y -> p (t y)"),
                                               in0=int_q[:, 0:n], scalar=float(-CH), in1=v,
                                               op0=ALU.mult, op1=ALU.add).then_inc(index_h_made, 1)

            def split(t, k):
                dve.wait_ge(piece_landed[k], 16 * t + 16)
                if k >= 2:
                    dve.wait_ge(mid_made, NP * t + k - 1)
                elif not isinstance(t, int) or t > 0:
                    dve.wait_ge(mid_made, NP * t)
                nc.vector.tensor_tensor(rest[:, k % 2, :], values[:, k % 3, :], values_hi[k % 3],
                                        ALU.subtract).then_inc(rest_made, 1)
                dve.wait_ge(rest_made, NP * t + k + 1)
                dve.wait_ge(piece_used, NP * t + k + 1)
                nc.vector.tensor_tensor(lo[:, k, :], rest[:, k % 2, :], rest_hi[k % 2],
                                        ALU.subtract).then_inc(lo_made, 1)

            def sum_slot(g, s):
                dve.wait_ge(landed[s], 16 * SLOT_ROWS * g + 16 * SLOT_ROWS)
                if not isinstance(g, int) or g < G - 1:
                    next_indices(g + 1, s)
                if not isinstance(g, int) or g > 0:
                    dve.wait_ge(bag_summed, g)
                nc.vector.tensor_reduce(slot_sum[:, s, :], rows[:, s, :, :].rearrange("p j e -> p e j"),
                                        axis=mybir.AxisListType.X, op=ALU.add).then_inc(slot_summed, 1)

            def one_hots(t, hb):
                if not (isinstance(t, int) and t == 0 and hb == 0):
                    dve.wait_ge(counted, (2 * t + hb) * STEPS)
                def of(index, n):
                    v = index[:, bass.ds(t, 1), hb * YP:(hb + 1) * YP] if not isinstance(t, int) \
                        else index[:, t:t + 1, hb * YP:(hb + 1) * YP]
                    return v.to_broadcast([P, n, YP])
                nc.vector.tensor_tensor(onehot_h[:], number[:, 0:CH, :], of(index_h, CH),
                                        ALU.is_equal).then_inc(onehot_h_made, 1)
                nc.vector.tensor_tensor(onehot_q[:], number[:], of(index_q, P),
                                        ALU.is_equal).then_inc(onehot_q_made, 1)

            def keep(t, hb, s):
                if s in ACT_STEPS:
                    return
                n = min(BS, Y - s * BS)
                dve.wait_ge(counted, (2 * t + hb) * STEPS + s + 1)
                nc.vector.tensor_copy(counts[hb][:, 2 * s * BS + 1:2 * (s * BS + n):2, :],
                                      ps_count[s % 2][1][:, 0:n * CH].rearrange("p (y h) -> p y h", h=CH)
                                      ).then_inc(kept[1], 1)

            def keep_sum(t, hb, upper):
                dve.wait_ge(part_kept, 2 * t + hb + 1)
                at = (2 * (t - TU * upper) + hb) * BH
                where = slice(D * upper, D * upper + D)
                dst = dense_sum[where, bass.ds(at, BH)] if not isinstance(t, int) else dense_sum[where, at:at + BH]
                nc.vector.scalar_tensor_tensor(out=dst, in0=ps_sum[hb][0:D, 0:BH], scalar=F8E3_ONE / J,
                                               in1=part_sum[D:P, hb, :], op0=ALU.mult, op1=ALU.add
                                               ).then_inc(half_kept, 1)

            find_qh(0)
            dve.wait_ge(index_h_made, 1)
            dve.wait_ge(index_q_made, 1)
            dve.wait_ge(number_made, 2)
            one_hots(0, 0)
            for t in range(2, TG):
                gather_indices(t)
            split(0, 0)
            for s in range(STEPS):
                keep(0, 0, s)
            one_hots(0, 1)
            dve.wait_ge(gather_idx_made, TG)
            sum_slot(0, 0)
            for k in range(1, EARLY):
                split(0, k)
            find_qh(1)
            find_qh(2)
            dve.wait_ge(index_h_made, 3)
            dve.wait_ge(index_q_made, 3)

            def table_steps(t, upper, last):
                for s in range(STEPS):
                    keep(t, 1, s)
                    if s in SPLIT_AFTER[0]:
                        split(t, EARLY + SPLIT_AFTER[0].index(s))
                    if s == SUM_AFTER[0]:
                        sum_slot(t, 1)
                if not last:
                    one_hots(t + 1, 0)
                keep_sum(t, 0, upper)
                if not last:
                    for s in range(STEPS):
                        keep(t + 1, 0, s)
                        if s in SPLIT_AFTER[1]:
                            split(t + 1, SPLIT_AFTER[1].index(s))
                        if s == SUM_AFTER[1]:
                            sum_slot(t + 1, 0)
                    one_hots(t + 1, 1)
                    for k in range(len(SPLIT_AFTER[1]), EARLY):
                        split(t + 1, k)
                else:
                    sum_slot(t + 1, 0)
                keep_sum(t, 1, upper)

            with dve.Fori(0, TU) as t:
                table_steps(t, 0, False)
            with dve.Fori(TU, TD - 1) as t:
                table_steps(t, 1, False)
            table_steps(TD - 1, 1, True)
            for g in range(TD, G):
                if g > TD:
                    sum_slot(g, 0)
                sum_slot(g, 1)

        @block.scalar
        def _(act):
            act.sem_inc(slot_summed, 2)
            act.sem_inc(bag_free, 1)
            act.sem_inc(half_kept, 2)
            act.sem_inc(piece_used, NP)
            act.wait_ge(numbers_made, 4)
            def numbers(n0, n1):
                nc.scalar.activation(number[:, n0:n1, :],
                                     n_no[:, n0:n1].rearrange("p (n a) -> p n a", a=1).to_broadcast([P, n1 - n0, YP]),
                                     ACT.Copy).then_inc(number_made, 1)

            numbers(0, P // 2)
            act.wait_ge(idx_landed, 16)
            act.wait_ge(choice_made, R6 + BT)
            for n in range(BT):
                for r in range(R6_DVE, R6):
                    c = 64 * (r // F) + J * (r % F)
                    nc.scalar.activation(spread[:, n, :, c:c + J],
                                         idx_in[:, n, 0:TD * J].rearrange("p (t j) -> p t j", t=TD), ACT.Copy,
                                         scale=residue[:, n, r:r + 1]).then_inc(spread_made, 1)
            numbers(P // 2, P)

            def keep_q(i):
                t0, t1, _ = INDEX_PARTS[i]
                act.wait_ge(q_made, i + 1)
                nc.scalar.activation(index_q[:, t0:t1, :].rearrange("p t y -> p (t y)"),
                                     int_q[:, 0:(t1 - t0) * 2 * YP], ACT.Copy).then_inc(index_q_made, 1)

            keep_q(0)

            def weigh(t, hb):
                act.wait_ge(onehot_h_made, 2 * t + hb + 1)
                nc.scalar.activation(onehot_h[:], onehot_h[:], ACT.Copy, scale=worth[:, 0:1]).then_inc(onehot_h_weighed, 1)

            def split(t, k):
                act.wait_ge(piece_landed[k], 16 * t + 16)
                act.wait_ge(piece_used, NP * t + k + 1)
                nc.scalar.activation(hi_mid[:, k, :, 0, :], values_hi[k % 3].rearrange("p (c d) -> p c d", d=D),
                                     ACT.Copy).then_inc(hi_made, 1)
                act.wait_ge(rest_made, NP * t + k + 1)
                nc.scalar.activation(hi_mid[:, k, :, 1, :], rest_hi[k % 2].rearrange("p (c d) -> p c d", d=D),
                                     ACT.Copy).then_inc(mid_made, 1)

            def keep(t, hb, s):
                n = min(BS, Y - s * BS)
                act.wait_ge(counted, (2 * t + hb) * STEPS + s + 1)
                for g in range(2 if s in ACT_STEPS else 1):
                    last = nc.scalar.activation(counts[hb][:, 2 * s * BS + g:2 * (s * BS + n) - 1 + g:2, :],
                                                ps_count[s % 2][g][:, 0:n * CH].rearrange("p (y h) -> p y h", h=CH),
                                                ACT.Copy)
                last.then_inc(kept[0], 1)

            def keep_sum(t, hb):
                if hb == 0:
                    act.wait_ge(half_summed, t + 1)
                else:
                    act.wait_ge(piece_used, NP * t + 2 * NP)
                act.wait_ge(half_kept, 2 * t + hb + 1)
                nc.scalar.activation(part_sum[D:P, hb, :], ps_sum[hb][D:P, 0:BH], ACT.Copy,
                                     scale=F8E3_ONE / J).then_inc(part_kept, 1)

            def keep_bag(g):
                act.wait_ge(bag_summed, g + 1)
                dst = gathered_sum[:, bass.ds(g * P, P)] if not isinstance(g, int) else gathered_sum[:, g * P:(g + 1) * P]
                nc.scalar.activation(dst, ps_bag[:, 0:P], ACT.Copy, scale=1.0 / J).then_inc(bag_free, 1)

            act.wait_ge(worth_made, 1)
            weigh(0, 0)
            split(0, 0)
            for s in range(STEPS):
                keep(0, 0, s)
            weigh(0, 1)
            for k in range(1, EARLY):
                split(0, k)
            keep_q(1)
            keep_q(2)

            def table_steps(t, last):
                for s in range(STEPS):
                    keep(t, 1, s)
                    if s in SPLIT_AFTER[0]:
                        split(t, EARLY + SPLIT_AFTER[0].index(s))
                if not last:
                    weigh(t + 1, 0)
                keep_sum(t, 0)
                if not last:
                    for s in range(STEPS):
                        keep(t + 1, 0, s)
                        if s in SPLIT_AFTER[1]:
                            split(t + 1, SPLIT_AFTER[1].index(s))
                    keep_bag(t)
                    weigh(t + 1, 1)
                    for k in range(len(SPLIT_AFTER[1]), EARLY):
                        split(t + 1, k)
                else:
                    keep_bag(t)
                keep_sum(t, 1)

            with act.Fori(0, TD - 1) as t:
                table_steps(t, False)
            table_steps(TD - 1, True)

            def layers(n, b0_, b1_):
                for m in range(M0):
                    act.wait_ge(h0_summed, n * M0 + m + 1)
                    nc.scalar.activation(h0[:, m, b0_:b1_], ps_h0[m][:, b0_:b1_], ACT.Relu,
                                         bias=bias0[:, m:m + 1]).then_inc(h0_ready, 1)
                for m in range(M1):
                    act.wait_ge(h1_summed, n * M1 + m + 1)
                    nc.scalar.activation(h1[:, m, b0_:b1_], ps_sum[m][:, b0_:b1_], ACT.Relu,
                                         bias=bias1[:, m:m + 1]).then_inc(h1_ready, 1)
                act.wait_ge(y_summed, n + 1)
                nc.scalar.activation(y[:, b0_:b1_], ps_y[0:1, b0_:b1_], ACT.Identity, bias=bias2[:]).then_inc(y_ready, 1)

            act.wait_ge(weights_landed, 16 * 5)
            for g in range(TD, G - 1):
                keep_bag(g)
            layers(0, 0, B - P)
            keep_bag(G - 1)
            layers(1, B - P, B)

        @block.tensor
        def _(pe):
            def turn_indices(i):
                t0, t1, bank = INDEX_PARTS[i]
                for t in range(t0, t1):
                    at = (t - t0) * 2 * YP
                    for n in range(BT):
                        last = nc.tensor.matmul(bank[:, at:at + 2 * YP], spread[:, n, t, :], choose_y[:, n, :],
                                                start=(n == 0), stop=(n == BT - 1))
                last.then_inc(turned, 1)

            pe.wait_ge(pads_zeroed, 2)
            pe.wait_ge(choice_made, R6 + BT)
            pe.wait_ge(spread_made, BT * R6)
            turn_indices(0)
            turn_indices(1)

            def count(t, hb, s):
                n = min(BS, Y - s * BS)
                if s == 0:
                    pe.wait_ge(onehot_h_weighed, 2 * t + hb + 1)
                    pe.wait_ge(onehot_q_made, 2 * t + hb + 1)
                if s >= 2:
                    pe.wait_ge(kept[0], (2 * t + hb) * STEPS + s - 1)
                    pe.wait_ge(kept[1], (2 * t + hb) * DVE_STEPS + s - 1 - sum(x <= s - 2 for x in ACT_STEPS))
                for yy in range(n):
                    for g in range(2):
                        last = nc.tensor.matmul(ps_count[s % 2][g][:, yy * CH:(yy + 1) * CH],
                                                onehot_q[64 * g:64 * g + F * J, :, s * BS + yy],
                                                onehot_h[64 * g:64 * g + F * J, :, s * BS + yy],
                                                start=True, stop=True)
                last.then_inc(counted, 1)

            def turn_bags(g):
                pe.wait_ge(slot_summed, 2 * g + 4)
                pe.wait_ge(bag_free, g + 1)
                for s in range(2):
                    last = nc.tensor.matmul(ps_bag[:, 0:P], slot_sum[:, s, :], identity[:],
                                            start=(s == 0), stop=(s == 1))
                last.then_inc(bag_summed, 1)

            def half(t, hb, following):
                for k, steps in zip(kept, (STEPS, DVE_STEPS)):
                    pe.wait_ge(k, (2 * t + hb + 1) * steps)
                    pe.sem_inc(pe_gate, 1)
                pe.wait_ge(half_kept, 2 * t + hb + 1)
                pe.sem_inc(pe_gate, 1)
                if hb == 1:
                    pe.wait_ge(index_h_made, len(INDEX_PARTS))
                    pe.sem_inc(pe_gate, 1)
                for k in range(NP):
                    if following is not None and 0 <= 2 * k - COUNT_AT < STEPS:
                        count(*following, 2 * k - COUNT_AT)
                    if hb == 0:
                        for made in (mid_made, lo_made):
                            pe.wait_ge(made, NP * t + k + 1)
                            pe.sem_inc(pe_gate, 1)
                    for c in range(PC):
                        nc.tensor.matmul(ps_sum[hb][:, 0:BH], hi_mid[:, k, c, :, :].rearrange("p a d -> p (a d)"),
                                         count_bytes[hb][:, :, k * PC + c, 0:F],
                                         start=(k == 0 and c == 0), stop=False)
                    if following is not None and 0 <= 2 * k + 1 - COUNT_AT < STEPS:
                        count(*following, 2 * k + 1 - COUNT_AT)
                    if hb == 1 and k == TURN_AT:
                        turn_bags(t)
                    for c in range(PC):
                        odd = c % 2
                        last = nc.tensor.matmul(ps_sum[hb][odd * D:(odd + 1) * D, 0:BH], lo[:, k, c * D:(c + 1) * D],
                                                count_bytes[hb][:, :, k * PC + c, 0:F],
                                                start=False, stop=(k == NP - 1 and c >= PC - 2))
                    if hb == 1:
                        last.then_inc(piece_used, 1)
                    elif k == NP - 1:
                        last.then_inc(half_summed, 1)

            pe.wait_ge(identity_made, 1)
            for s in range(STEPS):
                count(0, 0, s)
            turn_indices(2)

            with pe.Fori(0, TD - 1) as t:
                half(t, 0, (t, 1))
                half(t, 1, (t + 1, 0))
            half(TD - 1, 0, (TD - 1, 1))
            half(TD - 1, 1, None)

            pe.wait_ge(w0_landed, 16 * 3)
            pe.wait_ge(half_kept, 2 * TD + 2)
            for m in range(M0):
                for t in range(TU):
                    nc.tensor.matmul(ps_h0[m][:, 0:B], w0_dense[:, t, m * P:(m + 1) * P],
                                     dense_sum[:, t * 2 * BH:t * 2 * BH + B], start=(t == 0), stop=False)

            def add_group(g):
                c, n = g // BT, g % BT
                pe.wait_ge(bag_free, g + 2)
                for m in range(M0):
                    last = nc.tensor.matmul(ps_h0[m][:, n * P:(n + 1) * P], w0_gathered[:, c, m * P:(m + 1) * P],
                                            gathered_sum[:, g * P:(g + 1) * P], start=False, stop=(g >= G - 2),
                                            skip_group_check=(g == G - 1))
                    if g >= G - 2:
                        last.then_inc(h0_summed, 1)

            def layers(n, b0_, b1_):
                for m in range(M1):
                    for c in range(M0):
                        pe.wait_ge(h0_ready, n * M0 + c + 1)
                        last = nc.tensor.matmul(ps_sum[m][:, b0_:b1_], w1[:, c, m * P:(m + 1) * P],
                                                h0[:, c, b0_:b1_], start=(c == 0), stop=(c == M0 - 1))
                    last.then_inc(h1_summed, 1)
                for c in range(M1):
                    pe.wait_ge(h1_ready, n * M1 + c + 1)
                    last = nc.tensor.matmul(ps_y[0:1, b0_:b1_], w2[:, c:c + 1], h1[:, c, b0_:b1_],
                                            start=(c == 0), stop=(c == M1 - 1))
                last.then_inc(y_summed, 1)

            for g in range(TD):
                add_group(g)
            for g in range(TD, G - 1):
                turn_bags(g)
                add_group(g)
            pe.wait_ge(weights_landed, 16 * 5)
            layers(0, 0, B - P)
            turn_bags(G - 1)
            add_group(G - 1)
            layers(1, B - P, B)


_INS = ["r_idx", "L0_rec_emb", "L0_rec_W0", "L0_rec_b0", "L0_rec_W1", "L0_rec_b1", "L0_rec_W2", "L0_rec_b2"]


def kernel(**inputs):
    import numpy as _np
    import concourse.bacc as _bacc
    from concourse import mybir as _mybir
    from concourse.bass_utils import run_bass_kernel_spmd as _run

    nc = _bacc.Bacc("TRN2", target_bir_lowering=False, num_devices=1)
    arrays, args = {}, []
    for name in _INS:
        a = _np.ascontiguousarray(inputs[name])
        arrays[f"in_{name}"] = a
        args.append(nc.dram_tensor(f"in_{name}", a.shape, _mybir.dt.from_np(a.dtype), kind="ExternalInput").ap())
    n = inputs["r_idx"].shape[0]
    args.append(nc.dram_tensor("out_y", (n,), _mybir.dt.float32, kind="ExternalOutput").ap())
    embedding_bags_mlp(nc, *args)
    r = _run(nc, [arrays], core_ids=[0])
    return r.results[0]["out_y"]
```
